# Optimizing a Trainium2 kernel written in Bass

```python
import numpy as np
import jax
import jax.numpy as jnp

def _softmax(x, axis=-1):
    return jax.nn.softmax(x, axis=axis)

def _gelu(x):
    return jax.nn.gelu(x, approximate=True)

def _silu(x):
    return jax.nn.silu(x)

def _sigmoid(x):
    return jax.nn.sigmoid(x)

def _layernorm(x, axis=-1, eps=1e-05):
    m = jnp.mean(x, axis=axis, keepdims=True)
    v = jnp.var(x, axis=axis, keepdims=True)
    return (x - m) / jnp.sqrt(v + eps)

def _scatter_add(tgt, idx, src, axis=0):
    return tgt.at[idx].add(src)

def _segment_sum(src, seg, n):
    return jax.ops.segment_sum(src, seg, n)
kernel_name = 'mk_adaln_ffn_d1_seqx_r2_a36507'

def setup_inputs(seed: int=0):
    np.random.seed(seed)
    _w = jnp.asarray

    def _rec_inputs():
        import jax
        import jax.numpy as jnp
        _rk = jax.random.key(seed)
        x = -0.000125 + 0.9999 * jax.random.normal(jax.random.fold_in(_rk, 1), (4, 1024, 1024), jnp.float32)
        _lenS = 1024 - jax.random.randint(jax.random.fold_in(_rk, 7), (4,), 0, max(1, 1024 // 4) + 1, jnp.int32)
        _lenS2 = 1024 - jax.random.randint(jax.random.fold_in(_rk, 8), (4,), 0, max(1, 1024 // 4) + 1, jnp.int32)
        fside_BxSxS_0 = -1.52775e-05 + 0.999936 * jax.random.normal(jax.random.fold_in(_rk, 11), (4, 1024, 1024), jnp.float32)
        cond_512 = -5.03954e-05 + 1.00559 * jax.random.normal(jax.random.fold_in(_rk, 12), (4, 256), jnp.float32)
        return (x, fside_BxSxS_0, cond_512)
    x, fside_BxSxS_0, cond_512 = _rec_inputs()

    def _L0_cond_setup():
        import jax, jax.numpy as jnp
        from jax import lax
        import numpy as np
        B, T, C, TD = (8, 1024, 1024, 256)

        def _bi_wkv(r, k, v, w, u, time_emb):
            tf = jax.nn.sigmoid(jnp.sum(time_emb, axis=-1))[:, None, None]
            decay = jnp.exp(-jnp.exp(w.astype(jnp.float32)))[None, :] * (0.5 + 0.5 * tf[:, :, 0])
            kf = k.astype(jnp.float32)
            vf = v.astype(jnp.float32)
            ek = jnp.exp(jnp.minimum(kf, 30.0))
            ekv = ek * vf

            def step(carry, x):
                a, b = carry
                ekv_t, ek_t = x
                a = a * decay + ekv_t
                b = b * decay + ek_t
                return ((a, b), (a, b))
            ekv_t = jnp.swapaxes(ekv, 0, 1)
            ek_t = jnp.swapaxes(ek, 0, 1)
            init = (jnp.zeros_like(decay), jnp.zeros_like(decay))
            _, (nf, df) = lax.scan(step, init, (ekv_t, ek_t))
            _, (nb, db) = lax.scan(step, init, (ekv_t, ek_t), reverse=True)
            nf = jnp.swapaxes(nf, 0, 1)
            df = jnp.swapaxes(df, 0, 1)
            nb = jnp.swapaxes(nb, 0, 1)
            db = jnp.swapaxes(db, 0, 1)
            euk = jnp.exp(jnp.minimum(u.astype(jnp.float32)[None, None, :] + kf, 30.0))
            num = nf + nb - ekv + euk * vf
            den = df + db - ek + euk
            base = jax.nn.sigmoid(r.astype(jnp.float32)) * (num / jnp.maximum(den, 1e-08))
            out = base * (0.8 + 0.2 * tf)
            return out.astype(r.dtype)
        key = jax.random.key(seed)
        ks = jax.random.split(key, 6)
        return {'r': jax.random.normal(ks[0], (B, T, C), dtype=jnp.float32), 'k': jax.random.normal(ks[1], (B, T, C), dtype=jnp.float32), 'v': jax.random.normal(ks[2], (B, T, C), dtype=jnp.float32), 'w': jax.random.normal(ks[3], (C,), dtype=jnp.float32), 'u': jax.random.normal(ks[4], (C,), dtype=jnp.float32), 'time_emb': jax.random.normal(ks[5], (B, TD), dtype=jnp.float32)}
    _L0_cond_all = _L0_cond_setup()
    _L0_cond_in = {k: v for k, v in _L0_cond_all.items() if k in ('w', 'u')}
    del _L0_cond_all

    def _L0_ffn_setup():
        import jax, jax.numpy as jnp
        import numpy as np

        def binarize_weight(w):
            alpha = jnp.mean(jnp.abs(w), axis=tuple(range(1, w.ndim)), keepdims=True)
            bw = jnp.where(w >= 0, 1.0, -1.0) * alpha
            return jax.lax.stop_gradient(bw - w) + w
        key = jax.random.key(seed)
        k1, k2, k3 = jax.random.split(key, 3)
        in_features, out_features = (1024, 1024)
        x = jax.random.normal(k1, (8, 1024, in_features), dtype=jnp.float32)
        std = np.sqrt(2.0 / out_features).astype(np.float32)
        weight = jax.random.normal(k2, (out_features, in_features), dtype=jnp.float32) * std
        bias = jax.random.normal(k3, (out_features,), dtype=jnp.float32) * 0.01
        return {'x': x, 'weight': weight, 'bias': bias}
    _L0_ffn_all = _L0_ffn_setup()
    _L0_ffn_in = {k: v for k, v in _L0_ffn_all.items() if k in ('weight', 'bias')}
    del _L0_ffn_all
    return {'x': x, 'fside_BxSxS_0': fside_BxSxS_0, 'cond_512': cond_512, 'L0_cond_w': _L0_cond_in['w'], 'L0_cond_u': _L0_cond_in['u'], 'L0_ffn_weight': _L0_ffn_in['weight'], 'L0_ffn_bias': _L0_ffn_in['bias']}

def reference(x, fside_BxSxS_0, cond_512, L0_cond_w, L0_cond_u, L0_ffn_weight, L0_ffn_bias):
    import jax
    import jax.numpy as jnp

    def _L0_cond_ref(r, k, v, w, u, time_emb):
        import jax, jax.numpy as jnp
        from jax import lax
        import numpy as np
        B, T, C, TD = (8, 1024, 1024, 256)

        def _bi_wkv(r, k, v, w, u, time_emb):
            tf = jax.nn.sigmoid(jnp.sum(time_emb, axis=-1))[:, None, None]
            decay = jnp.exp(-jnp.exp(w.astype(jnp.float32)))[None, :] * (0.5 + 0.5 * tf[:, :, 0])
            kf = k.astype(jnp.float32)
            vf = v.astype(jnp.float32)
            ek = jnp.exp(jnp.minimum(kf, 30.0))
            ekv = ek * vf

            def step(carry, x):
                a, b = carry
                ekv_t, ek_t = x
                a = a * decay + ekv_t
                b = b * decay + ek_t
                return ((a, b), (a, b))
            ekv_t = jnp.swapaxes(ekv, 0, 1)
            ek_t = jnp.swapaxes(ek, 0, 1)
            init = (jnp.zeros_like(decay), jnp.zeros_like(decay))
            _, (nf, df) = lax.scan(step, init, (ekv_t, ek_t))
            _, (nb, db) = lax.scan(step, init, (ekv_t, ek_t), reverse=True)
            nf = jnp.swapaxes(nf, 0, 1)
            df = jnp.swapaxes(df, 0, 1)
            nb = jnp.swapaxes(nb, 0, 1)
            db = jnp.swapaxes(db, 0, 1)
            euk = jnp.exp(jnp.minimum(u.astype(jnp.float32)[None, None, :] + kf, 30.0))
            num = nf + nb - ekv + euk * vf
            den = df + db - ek + euk
            base = jax.nn.sigmoid(r.astype(jnp.float32)) * (num / jnp.maximum(den, 1e-08))
            out = base * (0.8 + 0.2 * tf)
            return out.astype(r.dtype)
        return _bi_wkv(r, k, v, w, u, time_emb)

    def _L0_ffn_ref(x, weight, bias):
        import jax, jax.numpy as jnp
        import numpy as np

        def binarize_weight(w):
            alpha = jnp.mean(jnp.abs(w), axis=tuple(range(1, w.ndim)), keepdims=True)
            bw = jnp.where(w >= 0, 1.0, -1.0) * alpha
            return jax.lax.stop_gradient(bw - w) + w
        bw = binarize_weight(weight)
        return jnp.einsum('bsi,oi->bso', x, bw) + bias
    x = x + _L0_ffn_ref(_L0_cond_ref(x, fside_BxSxS_0, fside_BxSxS_0, L0_cond_w, L0_cond_u, cond_512), L0_ffn_weight, L0_ffn_bias)
    return x

_drawn_inputs = setup_inputs


def setup_inputs(seed=0):
    import zlib

    import numpy as np

    out = dict(_drawn_inputs(seed))
    spreads = {}
    factors = {'L0_ffn_bias': 6.25}
    for name, (base, spread) in spreads.items():
        noise = np.random.default_rng([zlib.crc32(name.encode()), seed]).standard_normal(out[name].shape)
        drawn = base * np.exp(spread * noise) if base else spread * noise
        out[name] = jnp.asarray(drawn.astype(out[name].dtype))
    for name, factor in factors.items():
        out[name] = (out[name] * factor).astype(out[name].dtype)
    return out
```

```python
from contextlib import ExitStack

import concourse.bass as bass
from concourse import mybir
from concourse.alu_op_type import AluOpType as ALU

P = 128
F32 = mybir.dt.float32
F16 = mybir.dt.float16
ACT = mybir.ActivationFunctionType
AX = mybir.AxisListType

E30 = 10686474581524.463
DEN_MIN = 1e-8
LN_BIAS = 2.0 ** -60
S_MIN = 2.0 ** -40
HI_SCALE = 2.0 ** -4
LO_GAIN = 2.0 ** 11
SIGN = 0.5
SEED = 2


def bi_wkv_binary_ffn(nc, x, k, cond, w, u, weight, bias, out):
    B, T, C = x.shape
    CT = C // P
    TT = T // P
    H = 512
    NH = T // H
    TH = H // P
    N = B * CT
    LAG = CT + 1
    TD = cond.shape[1]
    assert T == C and NH == 2 and CT % 2 == 0

    def tile_of(a, n):
        return a.rearrange("b (q p) (c f) -> b c p q f", p=P, f=P)[n // CT, n % CT]

    with ExitStack() as ctx:
        def sb(name, shape, dt=F32):
            return ctx.enter_context(nc.sbuf_tensor(name, shape, dt))

        def ps(name, shape, dt=F32):
            return ctx.enter_context(nc.psum_tensor(name, shape, dt))

        def sem(name):
            return ctx.enter_context(nc.semaphore(name))

        k_nat = [sb(f"k_nat{p}", [P, TT, P]) for p in range(2)]
        x_nat = [sb(f"x_nat{p}", [P, TT, P]) for p in range(2)]
        ek = [sb(f"ek{p}", [P, T]) for p in range(2)]
        ekv = [sb(f"ekv{p}", [P, T]) for p in range(2)]
        euk = [sb(f"euk{p}", [P, T]) for p in range(2)]
        own = [sb(f"own{p}", [P, T]) for p in range(2)]
        rec = [sb(f"rec{p}", [P, T]) for p in range(2)]
        wkv = [sb(f"wkv{p}", [P, T]) for p in range(2)]
        y_fm = [sb(f"y_fm{p}", [P, T]) for p in range(2)]
        x_res = [sb(f"x_res{p}", [P, TT, P]) for p in range(2)]
        o_nat = [sb(f"o_nat{p}", [P, TT, P]) for p in range(2)]
        y_start = sb("y_start", [P, 2])
        acts = sb("acts", [P, 2, 2 * CT, T], F16)
        sgn = sb("sgn", [P, 2, CT, C], F16)
        w_nat = y_fm
        s_nat = [o_nat[p][:, 0:TT // 2, :].rearrange("p q f -> p (q f)").bitcast(F16) for p in range(2)]
        ident = sb("ident", [P, P])
        ident16 = sb("ident16", [P, P], F16)
        rows = sb("rows", [3 * CT, P])
        wub = sb("wub", [P, 3 * CT])
        condb = sb("condb", [P, B, TD])
        csum = sb("csum", [P, B])
        ecs = sb("ecs", [P, B])
        tf1 = sb("tf1", [P, B])
        tf = sb("tf", [P, B])
        half = sb("half", [P, B])
        gain = sb("gain", [P, B])
        ew = sb("ew", [P, CT])
        eew = sb("eew", [P, CT])
        dec = sb("dec", [P, N])
        onep = sb("onep", [P, N])
        onem = sb("onem", [P, N])
        scl = sb("scl", [P, N])
        back = sb("back", [P, N])
        ucol = sb("ucol", [P, N])
        bcol = sb("bcol", [P, N])
        asum = sb("asum", [P, CT])
        oscale = sb("oscale", [P, N])
        junk = sb("junk", [P, C])
        lnb = sb("lnb", [P, 1])
        two = sb("two", [P, 1])

        kT = ps("kT", [P, T])
        sT = ps("sT", [P, T])
        prod = ps("prod", [P, NH, H])
        yT = ps("yT", [P, TH, P])
        dec_ps = ps("dec_ps", [P, N])
        wT = prod[:, 0, :].bitcast(F16).rearrange("p (c f) -> p c f", c=CT)
        wub_ps = yT[:, :, :].rearrange("p q f -> p (q f)")[:, 0:3 * CT]

        s_par, s_cond, s_id, s_rows, s_dve, s_act, s_osc = (
            sem(a) for a in ("s_par", "s_cond", "s_id", "s_rows", "s_dve", "s_act", "s_osc"))
        k_in, x_in, r_in, w_in, o_out = ([sem(f"{a}{p}") for p in range(2)]
                                         for a in ("k_in", "x_in", "r_in", "w_in", "o_out"))
        st = {a: sem("d_" + a) for a in (
            "kT", "exps", "sig", "sT", "clamp", "ekv", "own", "Fd", "startd", "yd", "den", "ln", "rec",
            "chk", "two", "inv", "Fn", "startn", "yn", "num", "quot", "base", "hi", "lo",
            "prod", "ev", "yT0", "yT1", "yc0", "yc1", "res", "abs", "sgn", "wT", "wTc")}

        def seed(eng, *steps):
            for a in steps:
                eng.sem_inc(st[a], SEED)

        def done(eng, a, n):
            eng.wait_ge(st[a], n + 1 + SEED)

        def landed(eng, sems, n, p):
            eng.wait_ge(sems[p], (n - p) * 8 + 16)

        def run(eng, step):
            step(0, 0, wt=1, early=1, nxt=1, nxt2=1)
            step(1, 1, wt=1, early=1, nxt=1, nxt2=1, late=1)
            with eng.Fori(2, CT - 1, 2) as q:
                step(q, 0, wt=1, early=1, nxt=1, nxt2=1, late=1)
                step(q + 1, 1, wt=1, early=1, nxt=1, nxt2=1, late=1)
            step(CT, 0, early=1, nxt=1, nxt2=1, late=1)
            step(CT + 1, 1, early=1, nxt=1, nxt2=1, late=1, out=1)
            with eng.Fori(CT + 2, N - 3, 2) as q:
                step(q, 0, early=1, nxt=1, nxt2=1, late=1, out=1, outl=1)
                step(q + 1, 1, early=1, nxt=1, nxt2=1, late=1, out=1, outl=1)
            step(N - 2, 0, early=1, nxt=1, late=1, out=1, outl=1)
            step(N - 1, 1, early=1, late=1, out=1, outl=1)
            step(N, 0, late=1, out=1, outl=1)
            with eng.Fori(N + 1, N + LAG - 1, 2) as q:
                step(q, 1, out=1, outl=1)
                step(q + 1, 0, out=1, outl=1)
            step(N + LAG, 1, outl=1)

        block = ctx.enter_context(nc.Block())

        @block.sync
        def _(sp):
            for p in range(2):
                sp.sem_inc(o_out[p], 16)
            sp.dma_start(k_nat[0][:, :, :], tile_of(k, 0)).then_inc(k_in[0], 16)
            for i, a in enumerate((w, u, bias)):
                sp.dma_start(rows[i * CT:(i + 1) * CT, :], a.rearrange("(c p) -> c p", p=P)).then_inc(s_par, 16)
            sp.dma_start(condb[:, :, :].rearrange("p b d -> p (b d)"),
                         cond.rearrange("b d -> (b d)").partition_broadcast(P)).then_inc(s_cond, 16)
            sp.dma_start(k_nat[1][:, :, :], tile_of(k, 1)).then_inc(k_in[1], 16)
            for p in range(2):
                sp.dma_start(x_nat[p][:, :, :], tile_of(x, p)).then_inc(x_in[p], 16)

            def step(n, p, wt=0, early=0, nxt=0, nxt2=0, late=0, out=0, outl=0):
                m = n - LAG
                if wt:
                    done(sp, "sgn", n - 2)
                    done(sp, "abs", n - 2)
                    sp.dma_start(w_nat[p][:, :], weight.rearrange("(o p) i -> o p i", p=P)[n])\
                      .then_inc(w_in[p], 16)
                if nxt2:
                    done(sp, "kT", n)
                    sp.dma_start(k_nat[p][:, :, :], tile_of(k, n + 2)).then_inc(k_in[p], 16)
                if late and nxt:
                    done(sp, "sT", n - 1)
                    sp.dma_start(x_nat[1 - p][:, :, :], tile_of(x, n + 1)).then_inc(x_in[1 - p], 16)
                if out:
                    done(sp, "res", m - 2)
                    sp.dma_start(x_res[1 - p][:, :, :], tile_of(x, m)).then_inc(r_in[1 - p], 16)
                if outl:
                    done(sp, "res", m - 1)
                    sp.dma_start(tile_of(out_, m - 1), o_nat[p][:, :, :]).then_inc(o_out[p], 16)

            out_ = out
            run(sp, step)
            for p in range(2):
                sp.wait_ge(o_out[p], 16 * N // 2 + 16)

        @block.gpsimd
        def _(pool):
            seed(pool, "chk", "inv", "num", "res")
            pool.memset(ident[:, :], 1.0).then_inc(s_id, 1)
            pool.wait_ge(s_id, 1)
            pool.affine_select(out=ident[:, :], in_=ident[:, :], compare_op=ALU.is_equal, fill=0.0, base=0,
                               pattern=[[-1, P]], channel_multiplier=1).then_inc(s_id, 1)

            def step(n, p, wt=0, early=0, nxt=0, nxt2=0, late=0, out=0, outl=0):
                if early:
                    done(pool, "rec", n)
                    done(pool, "lo", n - 2)
                    pool.tensor_tensor(wkv[p][:, :], euk[p][:, :], rec[p][:, :], ALU.mult).then_inc(st["chk"], 1)
                    done(pool, "yn", n)
                    pool.tensor_tensor(ekv[p][:, :], own[p][:, :], ekv[p][:, :], ALU.add).then_inc(st["num"], 1)
                    done(pool, "two", n)
                    pool.tensor_tensor(wkv[p][:, :], wkv[p][:, :], rec[p][:, :], ALU.mult).then_inc(st["inv"], 1)
                if outl:
                    landed(pool, r_in, n - LAG - 1, p)
                    done(pool, "yc1", n - LAG - 1)
                    pool.tensor_tensor(o_nat[p][:, :, :], o_nat[p][:, :, :], x_res[p][:, :, :], ALU.add)\
                        .then_inc(st["res"], 1)

            run(pool, step)

        @block.tensor
        def _(pe):
            seed(pe, "kT", "sT", "prod", "yT0", "yT1", "wT")

            def turn(dst, src, what, one, q0=0):
                for q in range(src):
                    ins = pe.transpose(dst(q), what(q), one)
                return ins

            def k_turn(n, p):
                landed(pe, k_in, n, p)
                done(pe, "own", n - 1)
                turn(lambda q: kT[:, q * P:(q + 1) * P], TT, lambda q: k_nat[p][:, q, :],
                     ident[:, :]).then_inc(st["kT"], 1)

            def product(m, h):
                slot = (m // CT) % 2 * CT
                feat = m % CT * P
                for part in range(2):
                    for c in range(CT):
                        ins = pe.matmul(prod[:, h, :], sgn[:, part, c, bass.ds(feat, P)],
                                        acts[:, part, bass.ds(slot + c, 1), h * H:(h + 1) * H]
                                        .rearrange("p a t -> p (a t)"),
                                        start=(part == 0 and c == 0), stop=(part == 1 and c == CT - 1))
                if h == NH - 1:
                    ins.then_inc(st["prod"], 1)

            def y_turn(m, p, h):
                turn(lambda q: yT[:, q, :], TH, lambda q: y_fm[p][:, h * H + q * P:h * H + (q + 1) * P],
                     ident[:, :]).then_inc(st[f"yT{h}"], 1)

            pe.wait_ge(s_id, 2)
            k_turn(0, 0)
            pe.wait_ge(s_par, 48)
            pe.transpose(wub_ps, rows[:, :], ident[0:3 * CT, 0:3 * CT]).then_inc(s_rows, 1)

            def step(n, p, wt=0, early=0, nxt=0, nxt2=0, late=0, out=0, outl=0):
                m = n - LAG
                if out:
                    done(pe, "lo", n - 2 if (early or late) else N - 1)
                    done(pe, "ev", m - 1)
                    product(m, 0)
                if nxt:
                    k_turn(n + 1, 1 - p)
                if outl:
                    done(pe, "ev", m - 1)
                    done(pe, "yc1", m - 2)
                    y_turn(m - 1, p, 0)
                if late:
                    done(pe, "sig", n - 1)
                    done(pe, "base", n - 2)
                    turn(lambda q: sT[:, q * P:(q + 1) * P], TT, lambda q: x_nat[1 - p][:, q, :],
                         ident[:, :]).then_inc(st["sT"], 1)
                if out:
                    product(m, 1)
                if outl:
                    done(pe, "yc0", m - 1)
                    y_turn(m - 1, p, 1)
                if wt:
                    done(pe, "sgn", n)
                    done(pe, "wTc", n - 1)
                    turn(lambda c: wT[:, c, :], CT, lambda c: s_nat[p][:, c * P:(c + 1) * P],
                         ident16[:, :]).then_inc(st["wT"], 1)
                if not wt and not out:
                    done(pe, "wTc", CT - 1)

            run(pe, step)

        @block.scalar
        def _(act):
            seed(act, "exps", "sig", "ln", "rec", "two", "hi", "ev", "yc0", "yc1", "abs", "wTc")
            act.preload_act_table_set("natural_log_exp_and_others")
            act.wait_ge(s_dve, 3)
            act.activation(ecs[:, :], csum[:, :], ACT.Exp, scale=-1.0).then_inc(s_act, 1)
            act.wait_ge(s_dve, 4)
            act.activation(ew[:, :], wub[:, 0:CT], ACT.Exp).then_inc(s_act, 1)
            act.wait_ge(s_act, 2)
            act.activation(eew[:, :], ew[:, :], ACT.Exp, scale=-1.0).then_inc(s_act, 1)

            def exps(n, p):
                done(act, "kT", n)
                done(act, "den", n - 2)
                act.activation(ek[p][:, :], kT[:, :], ACT.Exp)
                done(act, "chk", n - 2)
                act.activation(euk[p][:, :], kT[:, :], ACT.Exp, bias=ucol[:, bass.ds(n, 1)])\
                   .then_inc(st["exps"], 1)

            def evac(m, p):
                act.wait_ge(s_osc, 1)
                done(act, "yT1", m - 2)
                done(act, "prod", m)
                act.activation(y_fm[p][:, :], prod[:, :, :].rearrange("p h t -> p (h t)"), ACT.Identity,
                               scale=oscale[:, bass.ds(m, 1)], bias=bcol[:, bass.ds(m, 1)])\
                   .then_inc(st["ev"], 1)

            def y_copy(m, p, h):
                if h == 0:
                    act.wait_ge(o_out[p], (m - p) * 8 + 16)
                done(act, f"yT{h}", m)
                act.copy(o_nat[p][:, h * TH:(h + 1) * TH, :], yT[:, :, :]).then_inc(st[f"yc{h}"], 1)

            act.wait_ge(s_dve, 6)
            exps(0, 0)

            def step(n, p, wt=0, early=0, nxt=0, nxt2=0, late=0, out=0, outl=0):
                m = n - LAG
                if outl:
                    y_copy(m - 1, p, 0)
                if nxt:
                    exps(n + 1, 1 - p)
                if wt:
                    landed(act, w_in, n, p)
                    done(act, "abs", n - 1)
                    act.activation(junk[:, :], w_nat[p][:, :], ACT.Abs, accum_out=asum[:, bass.ds(n, 1)])\
                       .then_inc(st["abs"], 1)
                if early:
                    done(act, "den", n)
                    done(act, "inv", n - 2)
                    act.activation(rec[p][:, :], euk[p][:, :], ACT.Ln, bias=lnb[:, 0:1]).then_inc(st["ln"], 1)
                    done(act, "ln", n)
                    act.activation(rec[p][:, :], rec[p][:, :], ACT.Exp, scale=-1.0).then_inc(st["rec"], 1)
                if outl:
                    y_copy(m - 1, p, 1)
                if late:
                    done(act, "base", n - 1)
                    if out:
                        done(act, "prod", m - 1)
                    act.mul(acts[:, 0, bass.ds((n - 1) % (2 * CT), 1), :].rearrange("p a t -> p (a t)"),
                            wkv[1 - p][:, :], 1.0 / LO_GAIN).then_inc(st["hi"], 1)
                if wt:
                    done(act, "wT", n)
                    act.mul(sgn[:, 0, :, bass.ds(n * P, P)], wT, 1.0)
                    act.mul(sgn[:, 1, :, bass.ds(n * P, P)], wT, 1.0 / LO_GAIN).then_inc(st["wTc"], 1)
                if out:
                    evac(m, 1 - p)
                if early:
                    done(act, "chk", n)
                    act.activation(wkv[p][:, :], wkv[p][:, :], ACT.Identity, scale=-1.0, bias=two[:, 0:1])\
                       .then_inc(st["two"], 1)
                if early and p == 0:
                    for i in range(2):
                        landed(act, x_in, n + i, i)
                        act.activation(x_nat[i][:, :, :], x_nat[i][:, :, :], ACT.Sigmoid).then_inc(st["sig"], 1)
                    act.preload_act_table_set("natural_log_exp_and_others")

            run(act, step)

        @block.vector
        def _(dve):
            seed(dve, "clamp", "ekv", "own", "Fd", "startd", "yd", "den", "Fn", "startn", "yn",
                 "quot", "base", "lo", "sgn")
            c = [0]

            def link(ins):
                c[0] += 1
                ins.then_inc(s_dve, 1)
                dve.wait_ge(s_dve, c[0])

            def per_batch(col):
                return col.unsqueeze(1).to_broadcast([P, B, CT])

            link(dve.memset(lnb[:, :], LN_BIAS))
            link(dve.memset(two[:, :], 2.0))
            dve.wait_ge(s_cond, 16)
            link(dve.tensor_reduce(csum[:, :], condb[:, :, :], AX.X, ALU.add))
            dve.wait_ge(s_rows, 1)
            link(dve.tensor_copy(wub[:, :], wub_ps))
            link(dve.tensor_copy(ucol[:, :].rearrange("p (b c) -> p b c", b=B), per_batch(wub[:, CT:2 * CT])))
            link(dve.tensor_copy(bcol[:, :].rearrange("p (b c) -> p b c", b=B), per_batch(wub[:, 2 * CT:3 * CT])))
            dve.wait_ge(s_act, 1)
            link(dve.tensor_scalar(tf1[:, :], ecs[:, :], 1.0, None, ALU.add))
            link(dve.reciprocal(tf[:, :], tf1[:, :]))
            link(dve.tensor_scalar(half[:, :], tf[:, :], 0.5, 0.5, ALU.mult, ALU.add))
            link(dve.tensor_scalar(gain[:, :], tf[:, :], 0.2 / HI_SCALE, 0.8 / HI_SCALE, ALU.mult, ALU.add))
            dve.wait_ge(s_act, 3)
            for b in range(B):
                link(dve.tensor_scalar(dec[:, b * CT:(b + 1) * CT], eew[:, :], half[:, b:b + 1], None, ALU.mult))
            link(dve.tensor_copy(dec_ps[:, :], dec[:, :]))
            link(dve.tensor_scalar(onep[:, :], dec[:, :], 1.0, None, ALU.add))
            link(dve.tensor_scalar(onem[:, :], dec[:, :], -1.0, 1.0, ALU.mult, ALU.add))
            link(dve.tensor_tensor(scl[:, :], onem[:, :], onep[:, :], ALU.mult))
            link(dve.tensor_scalar(scl[:, :], scl[:, :], S_MIN, None, ALU.max))
            link(dve.reciprocal(back[:, :], scl[:, :]))
            link(dve.tensor_tensor(back[:, :], back[:, :], dec[:, :], ALU.mult))
            dve.wait_ge(s_id, 2)
            link(dve.tensor_copy(ident16[:, :], ident[:, :]))

            def forward(buf, n, after, kind):
                done(dve, after, n)
                d = dec_ps[:, bass.ds(n, 1)].to_broadcast([P, T])
                dve.tensor_tensor_scan(buf, d, buf, 0.0, ALU.mult, ALU.add).then_inc(st["F" + kind], 1)

            def start_from(buf, n, kind):
                start = y_start[:, 0:1] if kind == "d" else y_start[:, 1:2]
                done(dve, "F" + kind, n)
                dve.tensor_tensor(start, buf[:, T - 1:T], back[:, bass.ds(n, 1)], ALU.mult)\
                   .then_inc(st["start" + kind], 1)

            def backward(buf, n, kind):
                d = dec_ps[:, bass.ds(n, 1)].to_broadcast([P, T])
                start = y_start[:, 0:1] if kind == "d" else y_start[:, 1:2]
                done(dve, "start" + kind, n)
                dve.tensor_tensor_scan(buf[:, ::-1], d, buf[:, ::-1], start, ALU.mult, ALU.add)\
                   .then_inc(st["y" + kind], 1)

            def step(n, p, wt=0, early=0, nxt=0, nxt2=0, late=0, out=0, outl=0):
                m = n - LAG
                col = bass.ds(n, 1)
                E, V, U, W = ek[p][:, :], ekv[p][:, :], euk[p][:, :], wkv[1 - p][:, :]
                if early:
                    done(dve, "exps", n)
                    dve.tensor_scalar(E, E, E30, scl[:, col], ALU.min, ALU.mult).then_inc(st["clamp"], 1)
                    dve.scalar_tensor_tensor(own[p][:, :], U, E30, kT[:, :], ALU.min, ALU.mult)
                    done(dve, "clamp", n)
                    dve.tensor_tensor(V, E, kT[:, :], ALU.mult).then_inc(st["own"], 1)
                    forward(E, n, "clamp", "d")
                if wt:
                    landed(dve, w_in, n, p)
                    done(dve, "wT", n - 2)
                    dve.tensor_scalar(s_nat[p], w_nat[p][:, :], 0.0, SIGN, ALU.is_ge, ALU.subtract)\
                       .then_inc(st["sgn"], 1)
                if early and not wt and not out:
                    done(dve, "abs", CT - 1)
                    for b in range(B):
                        ins = dve.tensor_scalar(oscale[:, b * CT:(b + 1) * CT], asum[:, :], gain[:, b:b + 1],
                                                1.0 / (C * SIGN), ALU.mult, ALU.mult)
                    ins.then_inc(s_osc, 1)
                if early:
                    start_from(E, n, "d")
                    backward(E, n, "d")
                if late:
                    done(dve, "inv", n - 1)
                    done(dve, "num", n - 1)
                    dve.scalar_tensor_tensor(W, W, 1.0 / DEN_MIN, ekv[1 - p][:, :], ALU.min, ALU.mult)\
                       .then_inc(st["quot"], 1)
                if early:
                    done(dve, "yd", n)
                    dve.scalar_tensor_tensor(U, U, E30, E, ALU.min, ALU.add).then_inc(st["den"], 1)
                if late:
                    done(dve, "sT", n - 1)
                    done(dve, "quot", n - 1)
                    dve.scalar_tensor_tensor(W, W, HI_SCALE * LO_GAIN, sT[:, :], ALU.mult, ALU.mult)\
                       .then_inc(st["base"], 1)
                if early:
                    forward(V, n, "own", "n")
                    start_from(V, n, "n")
                if early:
                    backward(V, n, "n")
                if late:
                    done(dve, "hi", n - 1)
                    slot = bass.ds((n - 1) % (2 * CT), 1)
                    dve.scalar_tensor_tensor(acts[:, 1, slot, :].rearrange("p a t -> p (a t)"),
                                             acts[:, 0, slot, :].rearrange("p a t -> p (a t)"), -LO_GAIN, W,
                                             ALU.mult, ALU.add).then_inc(st["lo"], 1)

            run(dve, step)


_INS = ["x", "fside_BxSxS_0", "cond_512", "L0_cond_w", "L0_cond_u", "L0_ffn_weight", "L0_ffn_bias"]
_OUTS = [((4, 1024, 1024), "float32")]


def kernel(**inputs):
    import numpy as _np
    import concourse.bacc as _bacc
    from concourse import mybir as _mybir
    from concourse.bass_utils import run_bass_kernel_spmd as _run

    nc = _bacc.Bacc("TRN2", target_bir_lowering=False, num_devices=1)
    arrays, args = {}, []
    for name in _INS:
        a = _np.ascontiguousarray(inputs[name])
        arrays[f"in_{name}_dram"] = a
        args.append(nc.dram_tensor(f"in_{name}_dram", a.shape, _mybir.dt.from_np(a.dtype), kind="ExternalInput").ap())
    for i, (shape, dtype) in enumerate(_OUTS):
        dt = _mybir.dt.from_np(_np.dtype(dtype))
        args.append(nc.dram_tensor(f"out_{i}_dram", shape, dt, kind="ExternalOutput").ap())
    bi_wkv_binary_ffn(nc, *args)
    r = _run(nc, [arrays], core_ids=[0])
    return r.results[0]["out_0_dram"]
```

```python
from contextlib import ExitStack

import concourse.bass as bass
from concourse import mybir
from concourse.alu_op_type import AluOpType as ALU

P = 128
F32 = mybir.dt.float32
F16 = mybir.dt.float16
ACT = mybir.ActivationFunctionType
AX = mybir.AxisListType

E30 = 10686474581524.463
DEN_MIN = 1e-8
LN_BIAS = 2.0 ** -60
S_MIN = 2.0 ** -40
HI_SCALE = 2.0 ** -4
LO_GAIN = 2.0 ** 11
SIGN = 0.5
SEED = 2


def bi_wkv_binary_ffn(nc, x, k, cond, w, u, weight, bias, out):
    B, T, C = x.shape
    CT = C // P
    TT = T // P
    H = 512
    NH = T // H
    TH = H // P
    N = B * CT
    LAG = CT + 1
    TD = cond.shape[1]
    NPART = 4
    NE = N - NPART
    PARTS, WHOLE = 1, 2
    assert T == C and NH == 2 and CT == 2 * NPART and NPART % 2 == 0

    def tile_of(a, n):
        return a.rearrange("b (q p) (c f) -> b c p q f", p=P, f=P)[n // CT, n % CT]

    with ExitStack() as ctx:
        def sb(name, shape, dt=F32):
            return ctx.enter_context(nc.sbuf_tensor(name, shape, dt))

        def ps(name, shape, dt=F32):
            return ctx.enter_context(nc.psum_tensor(name, shape, dt))

        def sem(name):
            return ctx.enter_context(nc.semaphore(name))

        k_nat = [sb(f"k_nat{p}", [P, TT, P]) for p in range(2)]
        x_nat = [sb(f"x_nat{p}", [P, TT, P]) for p in range(2)]
        ek = [sb(f"ek{p}", [P, T]) for p in range(2)]
        ekv = [sb(f"ekv{p}", [P, T]) for p in range(2)]
        euk = [sb(f"euk{p}", [P, T]) for p in range(2)]
        own = [sb(f"own{p}", [P, T]) for p in range(2)]
        rec = [sb(f"rec{p}", [P, T]) for p in range(2)]
        wkv = [sb(f"wkv{p}", [P, T]) for p in range(2)]
        y_fm = [sb(f"y_fm{p}", [P, T]) for p in range(2)]
        x_res = [sb(f"x_res{p}", [P, TT, P]) for p in range(2)]
        o_nat = [sb(f"o_nat{p}", [P, TT, P]) for p in range(2)]
        y_part = sb("y_part", [P, NPART, T])
        y_start = sb("y_start", [P, 2])
        acts = sb("acts", [P, 2, 2 * CT, T], F16)
        sgn = sb("sgn", [P, 2, CT, C], F16)
        w_nat = y_fm
        junk = x_res[0][:, :, :].rearrange("p q f -> p (q f)")
        s_nat = [o_nat[p][:, 0:TT // 2, :].rearrange("p q f -> p (q f)").bitcast(F16) for p in range(2)]
        ident = sb("ident", [P, P])
        ident16 = sb("ident16", [P, P], F16)
        rows = sb("rows", [3 * CT, P])
        wub = sb("wub", [P, 3 * CT])
        condb = sb("condb", [P, B, TD])
        csum = sb("csum", [P, B])
        ecs = sb("ecs", [P, B])
        tf1 = sb("tf1", [P, B])
        tf = sb("tf", [P, B])
        half = sb("half", [P, B])
        gain = sb("gain", [P, B])
        ew = sb("ew", [P, CT])
        eew = sb("eew", [P, CT])
        dec = sb("dec", [P, N])
        onep = sb("onep", [P, N])
        onem = sb("onem", [P, N])
        scl = sb("scl", [P, N])
        back = sb("back", [P, N])
        ucol = sb("ucol", [P, N])
        bcol = sb("bcol", [P, N])
        asum = sb("asum", [P, CT])
        oscale = sb("oscale", [P, N])
        lnb = sb("lnb", [P, 1])
        two = sb("two", [P, 1])

        kT = ps("kT", [P, T])
        sT = ps("sT", [P, T])
        prod = ps("prod", [P, NH, H])
        yT = ps("yT", [P, TH, P])
        dec_ps = ps("dec_ps", [P, N])
        wT = prod[:, 0, :].bitcast(F16).rearrange("p (c f) -> p c f", c=CT)
        wub_ps = yT[:, :, :].rearrange("p q f -> p (q f)")[:, 0:3 * CT]

        s_par, s_cond, s_id, s_rows, s_dve, s_act, s_osc = (
            sem(a) for a in ("s_par", "s_cond", "s_id", "s_rows", "s_dve", "s_act", "s_osc"))
        k_in, x_in, r_in, w_in, o_out = ([sem(f"{a}{p}") for p in range(2)]
                                         for a in ("k_in", "x_in", "r_in", "w_in", "o_out"))
        st = {a: sem("d_" + a) for a in (
            "kT", "exps", "sig", "sT", "clamp", "ekv", "own", "Fd", "startd", "yd", "den", "ln", "rec",
            "chk", "two", "inv", "Fn", "startn", "yn", "num", "quot", "base", "hi", "lo",
            "prod", "ev", "yT0", "yT1", "yc0", "yc1", "res", "abs", "sgn", "wT", "wTc")}

        def seed(eng, *steps):
            for a in steps:
                eng.sem_inc(st[a], SEED)

        def done(eng, a, n):
            eng.wait_ge(st[a], n + 1 + SEED)

        def landed(eng, sems, n, p):
            eng.wait_ge(sems[p], (n - p) * 8 + 16)

        def run(eng, step):
            step(0, 0, wt=1, early=1, nxt=1, nxt2=1)
            step(1, 1, wt=1, early=1, nxt=1, nxt2=1, late=1)
            with eng.Fori(2, CT - 1, 2) as q:
                step(q, 0, wt=1, early=1, nxt=1, nxt2=1, late=1)
                step(q + 1, 1, wt=1, early=1, nxt=1, nxt2=1, late=1)
            step(CT, 0, early=1, nxt=1, nxt2=1, late=1)
            step(CT + 1, 1, early=1, nxt=1, nxt2=1, late=1, out=1)
            with eng.Fori(CT + 2, NE - 1, 2) as q:
                step(q, 0, early=1, nxt=1, nxt2=1, late=1, out=1, outl=1)
                step(q + 1, 1, early=1, nxt=1, nxt2=1, late=1, out=1, outl=1)
            step(NE, 0, early=1, nxt=1, nxt2=1, late=1, out=1, outl=1)
            for i in range(3):
                step(NE + 1 + i, (i + 1) % 2, early=1, nxt=int(i < 2), nxt2=int(i < 1), late=1, out=1, outl=1,
                     half=i)
            step(N, 0, late=1, out=1, outl=1, half=3)
            with eng.Fori(N + 1, N + NPART, 2) as q:
                step(q, 1, out=1, outl=1, tail=PARTS)
                step(q + 1, 0, out=1, outl=1, tail=PARTS)
            with eng.Fori(N + 1 + NPART, N + LAG - 1, 2) as q:
                step(q, 1, out=1, outl=1, tail=WHOLE)
                step(q + 1, 0, out=1, outl=1, tail=WHOLE)
            step(N + LAG, 1, outl=1, tail=WHOLE)

        prods = [prod[:, :, :], kT[:, :].rearrange("p (h t) -> p h t", h=NH)]
        parts = sT[:, :].rearrange("p (h t) -> p h t", h=NH)
        yTs = [yT[:, :, :], sT[:, H:T].rearrange("p (q f) -> p q f", q=TH)]
        s_half, s_halfc = sem("s_half"), sem("s_halfc")

        block = ctx.enter_context(nc.Block())

        @block.sync
        def _(sp):
            for p in range(2):
                sp.sem_inc(o_out[p], 16)
            sp.dma_start(k_nat[0][:, :, :], tile_of(k, 0)).then_inc(k_in[0], 16)
            for i, a in enumerate((w, u, bias)):
                sp.dma_start(rows[i * CT:(i + 1) * CT, :], a.rearrange("(c p) -> c p", p=P)).then_inc(s_par, 16)
            sp.dma_start(condb[:, :, :].rearrange("p b d -> p (b d)"),
                         cond.rearrange("b d -> (b d)").partition_broadcast(P)).then_inc(s_cond, 16)
            sp.dma_start(k_nat[1][:, :, :], tile_of(k, 1)).then_inc(k_in[1], 16)
            for p in range(2):
                sp.dma_start(x_nat[p][:, :, :], tile_of(x, p)).then_inc(x_in[p], 16)

            def stored_ready(m, tail):
                done(sp, "res", N - LAG - 1 if tail else m)
                if tail:
                    done(sp, "yc0", m)
                    done(sp, "yc1", m)

            def step(n, p, wt=0, early=0, nxt=0, nxt2=0, late=0, out=0, outl=0, half=None, tail=0):
                m = n - LAG
                if wt:
                    done(sp, "sgn", n - 2)
                    done(sp, "abs", n - 2)
                    sp.dma_start(w_nat[p][:, :], weight.rearrange("(o p) i -> o p i", p=P)[n])\
                      .then_inc(w_in[p], 16)
                if early and not wt and not out:
                    done(sp, "abs", CT - 1)
                if nxt2:
                    done(sp, "kT", n)
                    sp.dma_start(k_nat[p][:, :, :], tile_of(k, n + 2)).then_inc(k_in[p], 16)
                if late and nxt:
                    done(sp, "sT", n - 1)
                    sp.dma_start(x_nat[1 - p][:, :, :], tile_of(x, n + 1)).then_inc(x_in[1 - p], 16)
                if out:
                    stored_ready(m - 2, tail)
                    sp.dma_start(x_res[1 - p][:, :, :], tile_of(x, m)).then_inc(r_in[1 - p], 16)
                if outl:
                    stored_ready(m - 1, tail)
                    sp.dma_start(tile_of(out_, m - 1), o_nat[p][:, :, :]).then_inc(o_out[p], 16)

            out_ = out
            run(sp, step)
            for p in range(2):
                sp.wait_ge(o_out[p], 16 * N // 2 + 16)

        @block.gpsimd
        def _(pool):
            seed(pool, "chk", "inv", "num", "res")
            pool.memset(ident[:, :], 1.0).then_inc(s_id, 1)
            pool.wait_ge(s_id, 1)
            pool.affine_select(out=ident[:, :], in_=ident[:, :], compare_op=ALU.is_equal, fill=0.0, base=0,
                               pattern=[[-1, P]], channel_multiplier=1).then_inc(s_id, 1)

            def step(n, p, wt=0, early=0, nxt=0, nxt2=0, late=0, out=0, outl=0, half=None, tail=0):
                if early:
                    done(pool, "rec", n)
                    done(pool, "lo", n - 2)
                    pool.tensor_tensor(wkv[p][:, :], euk[p][:, :], rec[p][:, :], ALU.mult).then_inc(st["chk"], 1)
                    done(pool, "yn", n)
                    pool.tensor_tensor(ekv[p][:, :], own[p][:, :], ekv[p][:, :], ALU.add).then_inc(st["num"], 1)
                    done(pool, "two", n)
                    pool.tensor_tensor(wkv[p][:, :], wkv[p][:, :], rec[p][:, :], ALU.mult).then_inc(st["inv"], 1)
                if outl and not tail:
                    landed(pool, r_in, n - LAG - 1, p)
                    done(pool, "yc1", n - LAG - 1)
                    pool.tensor_tensor(o_nat[p][:, :, :], o_nat[p][:, :, :], x_res[p][:, :, :], ALU.add)\
                        .then_inc(st["res"], 1)

            run(pool, step)

        @block.tensor
        def _(pe):
            seed(pe, "kT", "sT", "prod", "yT0", "yT1", "wT")

            def turn(dst, src, what, one, q0=0):
                for q in range(src):
                    ins = pe.transpose(dst(q), what(q), one)
                return ins

            def k_turn(n, p):
                landed(pe, k_in, n, p)
                done(pe, "own", n - 1)
                turn(lambda q: kT[:, q * P:(q + 1) * P], TT, lambda q: k_nat[p][:, q, :],
                     ident[:, :]).then_inc(st["kT"], 1)

            def product(m, h, dst, tiles=range(CT)):
                slot = (m // CT) % 2 * CT
                feat = m % CT * P
                for part in range(2):
                    for c in tiles:
                        ins = pe.matmul(dst[:, h, :], sgn[:, part, c, bass.ds(feat, P)],
                                        acts[:, part, bass.ds(slot + c, 1), h * H:(h + 1) * H]
                                        .rearrange("p a t -> p (a t)"),
                                        start=(part == 0 and c == tiles[0]), stop=(part == 1 and c == tiles[-1]))
                return ins

            def y_turn(m, p, h, dst):
                turn(lambda q: dst[:, q, :], TH, lambda q: y_fm[p][:, h * H + q * P:h * H + (q + 1) * P],
                     ident[:, :]).then_inc(st[f"yT{h}"], 1)

            pe.wait_ge(s_id, 2)
            k_turn(0, 0)
            pe.wait_ge(s_par, 48)
            pe.transpose(wub_ps, rows[:, :], ident[0:3 * CT, 0:3 * CT]).then_inc(s_rows, 1)

            def step(n, p, wt=0, early=0, nxt=0, nxt2=0, late=0, out=0, outl=0, half=None, tail=0):
                m = n - LAG
                bank = prods[p if tail else 0]
                tiles = range(NPART, CT) if tail == PARTS else range(CT)
                if out:
                    done(pe, "lo", N - 1 if tail else n - 2)
                    done(pe, "ev", m - 2 if tail else m - 1)
                    product(m, 0, bank, tiles)
                if nxt:
                    k_turn(n + 1, 1 - p)
                if outl:
                    done(pe, "ev", m - 1)
                    if tail:
                        done(pe, "yc0", m - 2)
                        pe.wait_ge(s_halfc, NPART)
                    done(pe, "yc1", m - 2)
                    y_turn(m - 1, p, 0, yTs[0])
                if late:
                    done(pe, "sig", n - 1)
                    done(pe, "base", n - 2)
                    if half:
                        pe.wait_ge(s_halfc, half)
                    turn(lambda q: sT[:, q * P:(q + 1) * P], TT, lambda q: x_nat[1 - p][:, q, :],
                         ident[:, :]).then_inc(st["sT"], 1)
                if out:
                    product(m, 1, bank, tiles).then_inc(st["prod"], 1)
                if outl:
                    if not tail:
                        done(pe, "yc0", m - 1)
                    y_turn(m - 1, p, 1, yTs[1 if tail else 0])
                if half is not None:
                    done(pe, "lo", NE - 1)
                    done(pe, "base", n - 1)
                    for h in range(NH):
                        ins = product(N - CT + half, h, parts, range(NPART))
                    ins.then_inc(s_half, 1)
                if wt:
                    done(pe, "sgn", n)
                    done(pe, "wTc", n - 1)
                    turn(lambda c: wT[:, c, :], CT, lambda c: s_nat[p][:, c * P:(c + 1) * P],
                         ident16[:, :]).then_inc(st["wT"], 1)
                if not wt and not out:
                    done(pe, "wTc", CT - 1)

            run(pe, step)

        @block.scalar
        def _(act):
            seed(act, "exps", "sig", "ln", "rec", "two", "hi", "ev", "yc0", "yc1", "abs", "wTc")
            act.preload_act_table_set("natural_log_exp_and_others")
            act.wait_ge(s_dve, 3)
            act.activation(ecs[:, :], csum[:, :], ACT.Exp, scale=-1.0).then_inc(s_act, 1)
            act.wait_ge(s_dve, 4)
            act.activation(ew[:, :], wub[:, 0:CT], ACT.Exp).then_inc(s_act, 1)
            act.wait_ge(s_act, 2)
            act.activation(eew[:, :], ew[:, :], ACT.Exp, scale=-1.0).then_inc(s_act, 1)

            def exps(n, p):
                done(act, "kT", n)
                done(act, "den", n - 2)
                act.activation(ek[p][:, :], kT[:, :], ACT.Exp)
                done(act, "chk", n - 2)
                act.activation(euk[p][:, :], kT[:, :], ACT.Exp, bias=ucol[:, bass.ds(n, 1)])\
                   .then_inc(st["exps"], 1)

            def evac(m, p, src):
                act.wait_ge(s_osc, 1)
                done(act, "yT1", m - 2)
                done(act, "prod", m)
                act.activation(y_fm[p][:, :], src.rearrange("p h t -> p (h t)"), ACT.Identity,
                               scale=oscale[:, bass.ds(m, 1)], bias=bcol[:, bass.ds(m, 1)])\
                   .then_inc(st["ev"], 1)

            def y_copy(m, p, h):
                if h == 0:
                    act.wait_ge(o_out[p], (m - p) * 8 + 16)
                done(act, f"yT{h}", m)
                act.copy(o_nat[p][:, h * TH:(h + 1) * TH, :], yT[:, :, :]).then_inc(st[f"yc{h}"], 1)

            act.wait_ge(s_dve, 6)
            exps(0, 0)

            def step(n, p, wt=0, early=0, nxt=0, nxt2=0, late=0, out=0, outl=0, half=None, tail=0):
                m = n - LAG
                if outl and not tail:
                    y_copy(m - 1, p, 0)
                if nxt:
                    exps(n + 1, 1 - p)
                if wt:
                    landed(act, w_in, n, p)
                    done(act, "abs", n - 1)
                    act.activation(junk, w_nat[p][:, :], ACT.Abs, accum_out=asum[:, bass.ds(n, 1)])\
                       .then_inc(st["abs"], 1)
                if early:
                    done(act, "den", n)
                    done(act, "inv", n - 2)
                    act.activation(rec[p][:, :], euk[p][:, :], ACT.Ln, bias=lnb[:, 0:1]).then_inc(st["ln"], 1)
                    done(act, "ln", n)
                    act.activation(rec[p][:, :], rec[p][:, :], ACT.Exp, scale=-1.0).then_inc(st["rec"], 1)
                if outl and not tail:
                    y_copy(m - 1, p, 1)
                if late:
                    done(act, "base", n - 1)
                    if out:
                        done(act, "prod", m - 1)
                    act.mul(acts[:, 0, bass.ds((n - 1) % (2 * CT), 1), :].rearrange("p a t -> p (a t)"),
                            wkv[1 - p][:, :], 1.0 / LO_GAIN).then_inc(st["hi"], 1)
                if wt:
                    done(act, "wT", n)
                    act.mul(sgn[:, 0, :, bass.ds(n * P, P)], wT, 1.0)
                    act.mul(sgn[:, 1, :, bass.ds(n * P, P)], wT, 1.0 / LO_GAIN).then_inc(st["wTc"], 1)
                if out and tail != PARTS:
                    evac(m, 1 - p, prods[p if tail else 0])
                if early:
                    done(act, "chk", n)
                    act.activation(wkv[p][:, :], wkv[p][:, :], ACT.Identity, scale=-1.0, bias=two[:, 0:1])\
                       .then_inc(st["two"], 1)
                if early and p == 0:
                    for i in range(2):
                        landed(act, x_in, n + i, i)
                        act.activation(x_nat[i][:, :, :], x_nat[i][:, :, :], ACT.Sigmoid).then_inc(st["sig"], 1)
                    act.preload_act_table_set("natural_log_exp_and_others")
                if half is not None:
                    mh = N - CT + half
                    act.wait_ge(s_half, half + 1)
                    act.activation(y_part[:, half, :], sT[:, :], ACT.Identity,
                                   scale=oscale[:, mh:mh + 1], bias=bcol[:, mh:mh + 1]).then_inc(s_halfc, 1)

            run(act, step)

        @block.vector
        def _(dve):
            seed(dve, "clamp", "ekv", "own", "Fd", "startd", "yd", "den", "Fn", "startn", "yn",
                 "quot", "base", "lo", "sgn")
            c = [0]

            def link(ins):
                c[0] += 1
                ins.then_inc(s_dve, 1)
                dve.wait_ge(s_dve, c[0])

            def per_batch(col):
                return col.unsqueeze(1).to_broadcast([P, B, CT])

            link(dve.memset(lnb[:, :], LN_BIAS))
            link(dve.memset(two[:, :], 2.0))
            dve.wait_ge(s_cond, 16)
            link(dve.tensor_reduce(csum[:, :], condb[:, :, :], AX.X, ALU.add))
            dve.wait_ge(s_rows, 1)
            link(dve.tensor_copy(wub[:, :], wub_ps))
            link(dve.tensor_copy(ucol[:, :].rearrange("p (b c) -> p b c", b=B), per_batch(wub[:, CT:2 * CT])))
            link(dve.tensor_copy(bcol[:, :].rearrange("p (b c) -> p b c", b=B), per_batch(wub[:, 2 * CT:3 * CT])))
            dve.wait_ge(s_act, 1)
            link(dve.tensor_scalar(tf1[:, :], ecs[:, :], 1.0, None, ALU.add))
            link(dve.reciprocal(tf[:, :], tf1[:, :]))
            link(dve.tensor_scalar(half[:, :], tf[:, :], 0.5, 0.5, ALU.mult, ALU.add))
            link(dve.tensor_scalar(gain[:, :], tf[:, :], 0.2 / HI_SCALE, 0.8 / HI_SCALE, ALU.mult, ALU.add))
            dve.wait_ge(s_act, 3)
            for b in range(B):
                link(dve.tensor_scalar(dec[:, b * CT:(b + 1) * CT], eew[:, :], half[:, b:b + 1], None, ALU.mult))
            link(dve.tensor_copy(dec_ps[:, :], dec[:, :]))
            link(dve.tensor_scalar(onep[:, :], dec[:, :], 1.0, None, ALU.add))
            link(dve.tensor_scalar(onem[:, :], dec[:, :], -1.0, 1.0, ALU.mult, ALU.add))
            link(dve.tensor_tensor(scl[:, :], onem[:, :], onep[:, :], ALU.mult))
            link(dve.tensor_scalar(scl[:, :], scl[:, :], S_MIN, None, ALU.max))
            link(dve.reciprocal(back[:, :], scl[:, :]))
            link(dve.tensor_tensor(back[:, :], back[:, :], dec[:, :], ALU.mult))
            dve.wait_ge(s_id, 2)
            link(dve.tensor_copy(ident16[:, :], ident[:, :]))

            def forward(buf, n, after, kind):
                done(dve, after, n)
                d = dec_ps[:, bass.ds(n, 1)].to_broadcast([P, T])
                dve.tensor_tensor_scan(buf, d, buf, 0.0, ALU.mult, ALU.add).then_inc(st["F" + kind], 1)

            def residual(m, p):
                done(dve, "res", N - LAG - 1)
                landed(dve, r_in, m, p)
                dve.wait_ge(o_out[p], (m - p) * 8 + 16)
                for h in range(NH):
                    q = slice(h * TH, (h + 1) * TH)
                    done(dve, f"yT{h}", m)
                    dve.tensor_tensor(o_nat[p][:, q, :], yTs[h], x_res[p][:, q, :], ALU.add)\
                       .then_inc(st[f"yc{h}"], 1)

            def start_from(buf, n, kind):
                start = y_start[:, 0:1] if kind == "d" else y_start[:, 1:2]
                done(dve, "F" + kind, n)
                dve.tensor_tensor(start, buf[:, T - 1:T], back[:, bass.ds(n, 1)], ALU.mult)\
                   .then_inc(st["start" + kind], 1)

            def backward(buf, n, kind):
                d = dec_ps[:, bass.ds(n, 1)].to_broadcast([P, T])
                start = y_start[:, 0:1] if kind == "d" else y_start[:, 1:2]
                done(dve, "start" + kind, n)
                dve.tensor_tensor_scan(buf[:, ::-1], d, buf[:, ::-1], start, ALU.mult, ALU.add)\
                   .then_inc(st["y" + kind], 1)

            def step(n, p, wt=0, early=0, nxt=0, nxt2=0, late=0, out=0, outl=0, half=None, tail=0):
                m = n - LAG
                col = bass.ds(n, 1)
                E, V, U, W = ek[p][:, :], ekv[p][:, :], euk[p][:, :], wkv[1 - p][:, :]
                if early:
                    done(dve, "exps", n)
                    dve.tensor_scalar(E, E, E30, scl[:, col], ALU.min, ALU.mult).then_inc(st["clamp"], 1)
                    dve.scalar_tensor_tensor(own[p][:, :], U, E30, kT[:, :], ALU.min, ALU.mult)
                    done(dve, "clamp", n)
                    dve.tensor_tensor(V, E, kT[:, :], ALU.mult).then_inc(st["own"], 1)
                    forward(E, n, "clamp", "d")
                if wt:
                    landed(dve, w_in, n, p)
                    done(dve, "wT", n - 2)
                    dve.tensor_scalar(s_nat[p], w_nat[p][:, :], 0.0, SIGN, ALU.is_ge, ALU.subtract)\
                       .then_inc(st["sgn"], 1)
                if early and not wt and not out:
                    done(dve, "abs", CT - 1)
                    for b in range(B):
                        ins = dve.tensor_scalar(oscale[:, b * CT:(b + 1) * CT], asum[:, :], gain[:, b:b + 1],
                                                1.0 / (C * SIGN), ALU.mult, ALU.mult)
                    ins.then_inc(s_osc, 1)
                if early:
                    start_from(E, n, "d")
                    backward(E, n, "d")
                if late:
                    done(dve, "inv", n - 1)
                    done(dve, "num", n - 1)
                    dve.scalar_tensor_tensor(W, W, 1.0 / DEN_MIN, ekv[1 - p][:, :], ALU.min, ALU.mult)\
                       .then_inc(st["quot"], 1)
                if early:
                    done(dve, "yd", n)
                    dve.scalar_tensor_tensor(U, U, E30, E, ALU.min, ALU.add).then_inc(st["den"], 1)
                if late:
                    done(dve, "sT", n - 1)
                    done(dve, "quot", n - 1)
                    dve.scalar_tensor_tensor(W, W, HI_SCALE * LO_GAIN, sT[:, :], ALU.mult, ALU.mult)\
                       .then_inc(st["base"], 1)
                if early:
                    forward(V, n, "own", "n")
                    start_from(V, n, "n")
                if early:
                    backward(V, n, "n")
                if outl and tail:
                    residual(m - 1, p)
                if out and tail == PARTS:
                    done(dve, "prod", m)
                    dve.wait_ge(s_halfc, NPART)
                    done(dve, "yT1", m - 2)
                    dve.scalar_tensor_tensor(y_fm[1 - p][:, :], prods[p].rearrange("p h t -> p (h t)"),
                                             oscale[:, bass.ds(m, 1)],
                                             y_part[:, bass.ds(m - (N - CT), 1), :].rearrange("p a t -> p (a t)"),
                                             ALU.mult, ALU.add).then_inc(st["ev"], 1)
                if late:
                    done(dve, "hi", n - 1)
                    slot = bass.ds((n - 1) % (2 * CT), 1)
                    dve.scalar_tensor_tensor(acts[:, 1, slot, :].rearrange("p a t -> p (a t)"),
                                             acts[:, 0, slot, :].rearrange("p a t -> p (a t)"), -LO_GAIN, W,
                                             ALU.mult, ALU.add).then_inc(st["lo"], 1)

            run(dve, step)


_INS = ["x", "fside_BxSxS_0", "cond_512", "L0_cond_w", "L0_cond_u", "L0_ffn_weight", "L0_ffn_bias"]
_OUTS = [((4, 1024, 1024), "float32")]


def kernel(**inputs):
    import numpy as _np
    import concourse.bacc as _bacc
    from concourse import mybir as _mybir
    from concourse.bass_utils import run_bass_kernel_spmd as _run

    nc = _bacc.Bacc("TRN2", target_bir_lowering=False, num_devices=1)
    arrays, args = {}, []
    for name in _INS:
        a = _np.ascontiguousarray(inputs[name])
        arrays[f"in_{name}_dram"] = a
        args.append(nc.dram_tensor(f"in_{name}_dram", a.shape, _mybir.dt.from_np(a.dtype), kind="ExternalInput").ap())
    for i, (shape, dtype) in enumerate(_OUTS):
        dt = _mybir.dt.from_np(_np.dtype(dtype))
        args.append(nc.dram_tensor(f"out_{i}_dram", shape, dt, kind="ExternalOutput").ap())
    bi_wkv_binary_ffn(nc, *args)
    r = _run(nc, [arrays], core_ids=[0])
    return r.results[0]["out_0_dram"]
```

```python
from contextlib import ExitStack

import concourse.bass as bass
from concourse import mybir
from concourse.alu_op_type import AluOpType as ALU

P = 128
F32 = mybir.dt.float32
F16 = mybir.dt.float16
ACT = mybir.ActivationFunctionType
AX = mybir.AxisListType

E30 = 10686474581524.463
DEN_MIN = 1e-8
LN_BIAS = 2.0 ** -60
S_MIN = 2.0 ** -40
HI_SCALE = 2.0 ** -4
LO_GAIN = 2.0 ** 11
SIGN = 0.5
SEED = 2


def bi_wkv_binary_ffn(nc, x, k, cond, w, u, weight, bias, out):
    B, T, C = x.shape
    CT = C // P
    TT = T // P
    H = 512
    NH = T // H
    TH = H // P
    N = B * CT
    LAG = CT + 1
    TD = cond.shape[1]
    NPART = 4
    NE = N - NPART
    PARTS, WHOLE = 1, 2
    assert T == C and NH == 2 and CT == 2 * NPART and NPART % 2 == 0

    def tile_of(a, n):
        return a.rearrange("b (q p) (c f) -> b c p q f", p=P, f=P)[n // CT, n % CT]

    with ExitStack() as ctx:
        def sb(name, shape, dt=F32):
            return ctx.enter_context(nc.sbuf_tensor(name, shape, dt))

        def ps(name, shape, dt=F32):
            return ctx.enter_context(nc.psum_tensor(name, shape, dt))

        def sem(name):
            return ctx.enter_context(nc.semaphore(name))

        k_nat = [sb(f"k_nat{p}", [P, TT, P]) for p in range(2)]
        x_nat = [sb(f"x_nat{p}", [P, TT, P]) for p in range(2)]
        ek = [sb(f"ek{p}", [P, T]) for p in range(2)]
        ekv = [sb(f"ekv{p}", [P, T]) for p in range(2)]
        euk = [sb(f"euk{p}", [P, T]) for p in range(2)]
        own = [sb(f"own{p}", [P, T]) for p in range(2)]
        rec = [sb(f"rec{p}", [P, T]) for p in range(2)]
        wkv = [sb(f"wkv{p}", [P, T]) for p in range(2)]
        y_fm = [sb(f"y_fm{p}", [P, T]) for p in range(2)]
        x_res = [sb(f"x_res{p}", [P, TT, P]) for p in range(2)]
        o_nat = [sb(f"o_nat{p}", [P, TT, P]) for p in range(2)]
        y_part = sb("y_part", [P, NPART, T])
        y_start = sb("y_start", [P, 2])
        acts = sb("acts", [P, 2, 2 * CT, T], F16)
        sgn = sb("sgn", [P, 2, CT, C], F16)
        w_nat = y_fm
        junk = x_res[0][:, :, :].rearrange("p q f -> p (q f)")
        s_nat = [o_nat[p][:, 0:TT // 2, :].rearrange("p q f -> p (q f)").bitcast(F16) for p in range(2)]
        ident = sb("ident", [P, P])
        ident16 = sb("ident16", [P, P], F16)
        rows = sb("rows", [3 * CT, P])
        wub = sb("wub", [P, 3 * CT])
        condb = sb("condb", [P, B, TD])
        csum = sb("csum", [P, B])
        ecs = sb("ecs", [P, B])
        tf1 = sb("tf1", [P, B])
        tf = sb("tf", [P, B])
        half = sb("half", [P, B])
        gain = sb("gain", [P, B])
        ew = sb("ew", [P, CT])
        eew = sb("eew", [P, CT])
        dec = sb("dec", [P, N])
        onem = sb("onem", [P, N])
        scl = sb("scl", [P, N])
        back = sb("back", [P, N])
        ucol = sb("ucol", [P, N])
        bcol = sb("bcol", [P, N])
        asum = sb("asum", [P, CT])
        oscale = sb("oscale", [P, N])
        lnb = sb("lnb", [P, 1])
        two = sb("two", [P, 1])

        kT = ps("kT", [P, T])
        sT = ps("sT", [P, T])
        prod = ps("prod", [P, NH, H])
        yT = ps("yT", [P, TH, P])
        dec_ps = ps("dec_ps", [P, N])
        wT = prod[:, 0, :].bitcast(F16).rearrange("p (c f) -> p c f", c=CT)
        wub_ps = yT[:, :, :].rearrange("p q f -> p (q f)")[:, 0:3 * CT]

        s_par, s_cond, s_id, s_rows, s_dve, s_act, s_osc = (
            sem(a) for a in ("s_par", "s_cond", "s_id", "s_rows", "s_dve", "s_act", "s_osc"))
        k_in, x_in, r_in, w_in, o_out = ([sem(f"{a}{p}") for p in range(2)]
                                         for a in ("k_in", "x_in", "r_in", "w_in", "o_out"))
        st = {a: sem("d_" + a) for a in (
            "kT", "exps", "sig", "sT", "clamp", "ekv", "own", "Fd", "startd", "yd", "den", "ln", "rec",
            "chk", "two", "inv", "Fn", "startn", "yn", "num", "quot", "base", "hi", "hib", "lo",
            "prod", "ev", "yT0", "yT1", "yc0", "yc1", "res", "abs", "sgn", "sgnl", "wT", "wTc")}

        def seed(eng, *steps):
            for a in steps:
                eng.sem_inc(st[a], SEED)

        def done(eng, a, n):
            eng.wait_ge(st[a], n + 1 + SEED)

        def landed(eng, sems, n, p):
            eng.wait_ge(sems[p], (n - p) * 8 + 16)

        def run(eng, step):
            step(0, 0, wt=1, early=1, nxt=1, nxt3=1)
            step(1, 1, wt=1, early=1, nxt=1, nxt3=1, late=1)
            with eng.Fori(2, CT - 1, 2) as q:
                step(q, 0, wt=1, early=1, nxt=1, nxt3=1, late=1)
                step(q + 1, 1, wt=1, early=1, nxt=1, nxt3=1, late=1)
            step(CT, 0, early=1, nxt=1, nxt3=1, late=1)
            step(CT + 1, 1, early=1, nxt=1, nxt3=1, late=1, out=1)
            with eng.Fori(CT + 2, NE - 1, 2) as q:
                step(q, 0, early=1, nxt=1, nxt3=1, late=1, out=1, outl=1)
                step(q + 1, 1, early=1, nxt=1, nxt3=1, late=1, out=1, outl=1)
            step(NE, 0, early=1, nxt=1, nxt3=1, late=1, out=1, outl=1)
            for i in range(3):
                step(NE + 1 + i, (i + 1) % 2, early=1, nxt=int(i < 2), late=1, out=1, outl=1,
                     half=i)
            step(N, 0, late=1, out=1, outl=1, half=3)
            with eng.Fori(N + 1, N + NPART, 2) as q:
                step(q, 1, out=1, outl=1, tail=PARTS)
                step(q + 1, 0, out=1, outl=1, tail=PARTS)
            with eng.Fori(N + 1 + NPART, N + LAG - 1, 2) as q:
                step(q, 1, out=1, outl=1, tail=WHOLE)
                step(q + 1, 0, out=1, outl=1, tail=WHOLE)
            step(N + LAG, 1, outl=1, tail=WHOLE)

        prods = [prod[:, :, :], kT[:, :].rearrange("p (h t) -> p h t", h=NH)]
        parts = [bank[:, :] for bank in (sT, sT, kT, sT)]
        yTs = [yT[:, :, :], sT[:, H:T].rearrange("p (q f) -> p q f", q=TH)]
        s_half, s_halfc = sem("s_half"), sem("s_halfc")

        block = ctx.enter_context(nc.Block())

        @block.sync
        def _(sp):
            for p in range(2):
                sp.sem_inc(o_out[p], 16)
            sp.dma_start(k_nat[0][:, :, :], tile_of(k, 0)).then_inc(k_in[0], 16)
            for i, a in enumerate((w, u, bias)):
                sp.dma_start(rows[i * CT:(i + 1) * CT, :], a.rearrange("(c p) -> c p", p=P)).then_inc(s_par, 16)
            sp.dma_start(condb[:, :, :].rearrange("p b d -> p (b d)"),
                         cond.rearrange("b d -> (b d)").partition_broadcast(P)).then_inc(s_cond, 16)
            sp.dma_start(k_nat[1][:, :, :], tile_of(k, 1)).then_inc(k_in[1], 16)
            for p in range(2):
                sp.dma_start(x_nat[p][:, :, :], tile_of(x, p)).then_inc(x_in[p], 16)

            def stored_ready(m, tail):
                done(sp, "res", N - LAG - 1 if tail else m)
                if tail:
                    done(sp, "yc0", m)
                    done(sp, "yc1", m)

            def step(n, p, wt=0, early=0, nxt=0, nxt3=0, late=0, out=0, outl=0, half=None, tail=0):
                m = n - LAG
                if wt:
                    done(sp, "sgn", n - 2)
                    done(sp, "abs", n - 2)
                    sp.dma_start(w_nat[p][:, :], weight.rearrange("(o p) i -> o p i", p=P)[n])\
                      .then_inc(w_in[p], 16)
                if early and not wt and not out:
                    done(sp, "abs", CT - 1)
                if out:
                    stored_ready(m - 2, tail)
                    sp.dma_start(x_res[1 - p][:, :, :], tile_of(x, m)).then_inc(r_in[1 - p], 16)
                if outl:
                    stored_ready(m - 1, tail)
                    sp.dma_start(tile_of(out_, m - 1), o_nat[p][:, :, :]).then_inc(o_out[p], 16)

            out_ = out
            run(sp, step)
            for p in range(2):
                sp.wait_ge(o_out[p], 16 * N // 2 + 16)

        @block.gpsimd
        def _(pool):
            seed(pool, "chk", "inv", "num", "lo", "res")
            pool.memset(ident[:, :], 1.0).then_inc(s_id, 1)
            pool.wait_ge(s_id, 1)
            pool.affine_select(out=ident[:, :], in_=ident[:, :], compare_op=ALU.is_equal, fill=0.0, base=0,
                               pattern=[[-1, P]], channel_multiplier=1).then_inc(s_id, 1)

            def step(n, p, wt=0, early=0, nxt=0, nxt3=0, late=0, out=0, outl=0, half=None, tail=0):
                if early:
                    done(pool, "rec", n)
                    done(pool, "lo", n - 2)
                    pool.tensor_tensor(wkv[p][:, :], euk[p][:, :], rec[p][:, :], ALU.mult).then_inc(st["chk"], 1)
                    done(pool, "yn", n)
                    pool.tensor_tensor(ekv[p][:, :], own[p][:, :], ekv[p][:, :], ALU.add).then_inc(st["num"], 1)
                    done(pool, "two", n)
                    pool.tensor_tensor(wkv[p][:, :], wkv[p][:, :], rec[p][:, :], ALU.mult).then_inc(st["inv"], 1)
                if late:
                    done(pool, "hib", n - 1)
                    slot = bass.ds((n - 1) % (2 * CT), 1)
                    pool.tensor_tensor(acts[:, 1, slot, :].rearrange("p a t -> p (a t)"), wkv[1 - p][:, :],
                                       rec[1 - p][:, :], ALU.subtract).then_inc(st["lo"], 1)
                if outl and not tail:
                    landed(pool, r_in, n - LAG - 1, p)
                    done(pool, "yc1", n - LAG - 1)
                    pool.tensor_tensor(o_nat[p][:, :, :], o_nat[p][:, :, :], x_res[p][:, :, :], ALU.add)\
                        .then_inc(st["res"], 1)

            run(pool, step)

        @block.tensor
        def _(pe):
            seed(pe, "kT", "sT", "prod", "yT0", "yT1", "wT")

            def turn(dst, src, what, one):
                for q in range(src):
                    ins = pe.transpose(dst(q), what(q), one)
                return ins

            def k_turn(n, p):
                landed(pe, k_in, n, p)
                done(pe, "own", n - 1)
                turn(lambda q: kT[:, q * P:(q + 1) * P], TT, lambda q: k_nat[p][:, q, :],
                     ident[:, :]).then_inc(st["kT"], 1)

            def product(m, h, dst, tiles=range(CT)):
                slot = (m // CT) % 2 * CT
                feat = m % CT * P
                for part in range(2):
                    for c in tiles:
                        ins = pe.matmul(dst[:, h, :], sgn[:, part, c, bass.ds(feat, P)],
                                        acts[:, part, bass.ds(slot + c, 1), h * H:(h + 1) * H]
                                        .rearrange("p a t -> p (a t)"),
                                        start=(part == 0 and c == tiles[0]), stop=(part == 1 and c == tiles[-1]))
                return ins

            def y_turn(m, p, h, dst):
                turn(lambda q: dst[:, q, :], TH, lambda q: y_fm[p][:, h * H + q * P:h * H + (q + 1) * P],
                     ident[:, :]).then_inc(st[f"yT{h}"], 1)

            pe.wait_ge(s_id, 2)
            k_turn(0, 0)
            pe.wait_ge(s_par, 48)
            pe.transpose(wub_ps, rows[:, :], ident[0:3 * CT, 0:3 * CT]).then_inc(s_rows, 1)

            def step(n, p, wt=0, early=0, nxt=0, nxt3=0, late=0, out=0, outl=0, half=None, tail=0):
                m = n - LAG
                bank = prods[p if tail else 0]
                tiles = range(NPART, CT) if tail == PARTS else range(CT)

                def first_product():
                    done(pe, "lo", N - 1 if tail else (m // CT) * CT + CT - 1)
                    done(pe, "ev", m - 2 if tail else m - 1)
                    product(m, 0, bank, tiles)

                if nxt:
                    k_turn(n + 1, 1 - p)
                if late:
                    done(pe, "sig", n - 1)
                    done(pe, "base", n - 2)
                    if half in (1, 2):
                        pe.wait_ge(s_halfc, half)
                    turn(lambda q: sT[:, q * P:(q + 1) * P], TT, lambda q: x_nat[1 - p][:, q, :],
                         ident[:, :]).then_inc(st["sT"], 1)
                if tail and out:
                    first_product()
                if outl:
                    done(pe, "ev", m - 1)
                    if tail:
                        done(pe, "yc0", m - 2)
                        pe.wait_ge(s_halfc, NPART)
                    done(pe, "yc1", m - 2)
                    y_turn(m - 1, p, 0, yTs[0])
                if out and not tail:
                    first_product()
                if tail and out:
                    product(m, 1, bank, tiles).then_inc(st["prod"], 1)
                if outl:
                    if not tail:
                        done(pe, "yc0", m - 1)
                    y_turn(m - 1, p, 1, yTs[1 if tail else 0])
                if out and not tail:
                    product(m, 1, bank, tiles).then_inc(st["prod"], 1)
                if half is not None:
                    done(pe, "lo", NE - 1)
                    if half == 2:
                        done(pe, "own", n)
                    else:
                        done(pe, "base", n - 1)
                    dst = parts[half].rearrange("p (h t) -> p h t", h=NH)
                    for h in range(NH):
                        ins = product(N - CT + half, h, dst, range(NPART))
                    ins.then_inc(s_half, 1)
                if wt:
                    done(pe, "sgn", n)
                    done(pe, "wTc", n - 1)
                    turn(lambda c: wT[:, c, :], CT, lambda c: s_nat[p][:, c * P:(c + 1) * P],
                         ident16[:, :]).then_inc(st["wT"], 1)
                if not wt and not out:
                    done(pe, "sgnl", CT - 1)

            run(pe, step)

        @block.scalar
        def _(act):
            seed(act, "exps", "sig", "ln", "rec", "two", "hi", "hib", "ev", "yc0", "yc1", "abs", "wTc")
            act.preload_act_table_set("natural_log_exp_and_others")
            act.wait_ge(s_dve, 4)
            act.activation(ecs[:, :], csum[:, :], ACT.Exp, scale=-1.0).then_inc(s_act, 1)
            act.wait_ge(s_dve, 5)
            act.activation(ew[:, :], wub[:, 0:CT], ACT.Exp).then_inc(s_act, 1)
            act.wait_ge(s_act, 2)
            act.activation(eew[:, :], ew[:, :], ACT.Exp, scale=-1.0).then_inc(s_act, 1)

            def exps(n, p, more=True):
                done(act, "kT", n)
                done(act, "den", n - 2)
                act.activation(ek[p][:, :], kT[:, :], ACT.Exp)
                done(act, "chk", n - 2)
                act.activation(euk[p][:, :], kT[:, :], ACT.Exp, bias=ucol[:, bass.ds(n, 1)])\
                   .then_inc(st["exps"], 1)
                if more:
                    act.dma_start(k_nat[p][:, :, :], tile_of(k, n + 2)).then_inc(k_in[p], 16)

            def evac(m, p, src):
                act.wait_ge(s_osc, 1)
                done(act, "yT1", m - 2)
                done(act, "prod", m)
                act.activation(y_fm[p][:, :], src.rearrange("p h t -> p (h t)"), ACT.Identity,
                               scale=oscale[:, bass.ds(m, 1)], bias=bcol[:, bass.ds(m, 1)])\
                   .then_inc(st["ev"], 1)

            def part_copy(i):
                mh = N - CT + i
                act.wait_ge(s_half, i + 1)
                act.activation(y_part[:, i, :], parts[i], ACT.Identity,
                               scale=oscale[:, mh:mh + 1], bias=bcol[:, mh:mh + 1]).then_inc(s_halfc, 1)

            def y_copy(m, p, h):
                if h == 0:
                    act.wait_ge(o_out[p], (m - p) * 8 + 16)
                done(act, f"yT{h}", m)
                act.copy(o_nat[p][:, h * TH:(h + 1) * TH, :], yT[:, :, :]).then_inc(st[f"yc{h}"], 1)

            act.wait_ge(s_dve, 7)
            exps(0, 0)

            def step(n, p, wt=0, early=0, nxt=0, nxt3=0, late=0, out=0, outl=0, half=None, tail=0):
                m = n - LAG
                if outl and not tail and not half:
                    evac(m - 1, p, prods[0])
                if nxt:
                    exps(n + 1, 1 - p, more=nxt3)
                if outl and not tail:
                    y_copy(m - 1, p, 0)
                if late and nxt:
                    done(act, "sT", n - 1)
                    act.dma_start(x_nat[1 - p][:, :, :], tile_of(x, n + 1)).then_inc(x_in[1 - p], 16)
                if wt:
                    landed(act, w_in, n, p)
                    done(act, "abs", n - 1)
                    act.activation(junk, w_nat[p][:, :], ACT.Abs, accum_out=asum[:, bass.ds(n, 1)])\
                       .then_inc(st["abs"], 1)
                if early:
                    done(act, "den", n)
                    done(act, "lo", n - 2)
                    act.activation(rec[p][:, :], euk[p][:, :], ACT.Ln, bias=lnb[:, 0:1]).then_inc(st["ln"], 1)
                    done(act, "ln", n)
                    act.activation(rec[p][:, :], rec[p][:, :], ACT.Exp, scale=-1.0).then_inc(st["rec"], 1)
                if late:
                    done(act, "base", n - 1)
                    if out:
                        done(act, "prod", m - 1)
                    high = acts[:, 0, bass.ds((n - 1) % (2 * CT), 1), :].rearrange("p a t -> p (a t)")
                    act.mul(high, wkv[1 - p][:, :], 1.0 / LO_GAIN).then_inc(st["hi"], 1)
                if early and p == 0:
                    landed(act, x_in, n, 0)
                    act.activation(x_nat[0][:, :, :], x_nat[0][:, :, :], ACT.Sigmoid).then_inc(st["sig"], 1)
                if outl and not tail:
                    y_copy(m - 1, p, 1)
                if wt:
                    done(act, "wT", n)
                    act.mul(sgn[:, 0, :, bass.ds(n * P, P)], wT, 1.0).then_inc(st["wTc"], 1)
                if early:
                    done(act, "hi", n - 1)
                    done(act, "chk", n)
                    act.activation(wkv[p][:, :], wkv[p][:, :], ACT.Identity, scale=-1.0, bias=two[:, 0:1])\
                       .then_inc(st["two"], 1)
                if late:
                    if not early:
                        done(act, "hi", n - 1)
                    act.mul(rec[1 - p][:, :], high, LO_GAIN).then_inc(st["hib"], 1)
                if early and p == 0:
                    landed(act, x_in, n + 1, 1)
                    act.activation(x_nat[1][:, :, :], x_nat[1][:, :, :], ACT.Sigmoid).then_inc(st["sig"], 1)
                    act.preload_act_table_set("natural_log_exp_and_others")
                if half == 1:
                    part_copy(half)
                if out and (tail == WHOLE or half is not None):
                    evac(m, 1 - p, prods[p if tail else 0])
                if half in (0, 2, 3):
                    part_copy(half)

            run(act, step)

        @block.vector
        def _(dve):
            seed(dve, "clamp", "ekv", "own", "Fd", "startd", "yd", "den", "Fn", "startn", "yn",
                 "quot", "base", "sgn", "sgnl")
            c = [0]

            def link(ins):
                c[0] += 1
                ins.then_inc(s_dve, 1)
                dve.wait_ge(s_dve, c[0])

            def per_batch(col):
                return col.unsqueeze(1).to_broadcast([P, B, CT])

            dve.wait_ge(s_id, 2)
            link(dve.tensor_copy(ident16[:, :], ident[:, :]))
            link(dve.memset(lnb[:, :], LN_BIAS))
            link(dve.memset(two[:, :], 2.0))
            dve.wait_ge(s_cond, 16)
            link(dve.tensor_reduce(csum[:, :], condb[:, :, :], AX.X, ALU.add))
            dve.wait_ge(s_rows, 1)
            link(dve.tensor_copy(wub[:, :], wub_ps))
            link(dve.tensor_copy(ucol[:, :].rearrange("p (b c) -> p b c", b=B), per_batch(wub[:, CT:2 * CT])))
            link(dve.tensor_copy(bcol[:, :].rearrange("p (b c) -> p b c", b=B), per_batch(wub[:, 2 * CT:3 * CT])))
            dve.wait_ge(s_act, 1)
            link(dve.tensor_scalar(tf1[:, :], ecs[:, :], 1.0, None, ALU.add))
            link(dve.reciprocal(tf[:, :], tf1[:, :]))
            link(dve.tensor_scalar(half[:, :], tf[:, :], 0.5, 0.5, ALU.mult, ALU.add))
            link(dve.tensor_scalar(gain[:, :], tf[:, :], 0.2 / HI_SCALE, 0.8 / HI_SCALE, ALU.mult, ALU.add))
            dve.wait_ge(s_act, 3)
            for b in range(B):
                link(dve.tensor_scalar(dec[:, b * CT:(b + 1) * CT], eew[:, :], half[:, b:b + 1], None, ALU.mult))
            link(dve.tensor_copy(dec_ps[:, :], dec[:, :]))
            link(dve.tensor_scalar(onem[:, :], dec[:, :], -1.0, 1.0, ALU.mult, ALU.add))
            link(dve.scalar_tensor_tensor(scl[:, :], dec[:, :], 1.0, onem[:, :], ALU.add, ALU.mult))
            link(dve.tensor_scalar(scl[:, :], scl[:, :], S_MIN, None, ALU.max))
            link(dve.reciprocal(back[:, :], scl[:, :]))
            link(dve.tensor_tensor(back[:, :], back[:, :], dec[:, :], ALU.mult))
            def forward(buf, n, after, kind):
                done(dve, after, n)
                d = dec_ps[:, bass.ds(n, 1)].to_broadcast([P, T])
                dve.tensor_tensor_scan(buf, d, buf, 0.0, ALU.mult, ALU.add).then_inc(st["F" + kind], 1)

            def residual(m, p, h):
                if h == 0:
                    done(dve, "res", N - LAG - 1)
                    landed(dve, r_in, m, p)
                    dve.wait_ge(o_out[p], (m - p) * 8 + 16)
                q = slice(h * TH, (h + 1) * TH)
                done(dve, f"yT{h}", m)
                dve.tensor_tensor(o_nat[p][:, q, :], yTs[h], x_res[p][:, q, :], ALU.add)\
                   .then_inc(st[f"yc{h}"], 1)

            def start_from(buf, n, kind):
                start = y_start[:, 0:1] if kind == "d" else y_start[:, 1:2]
                done(dve, "F" + kind, n)
                dve.tensor_tensor(start, buf[:, T - 1:T], back[:, bass.ds(n, 1)], ALU.mult)\
                   .then_inc(st["start" + kind], 1)

            def backward(buf, n, kind):
                d = dec_ps[:, bass.ds(n, 1)].to_broadcast([P, T])
                start = y_start[:, 0:1] if kind == "d" else y_start[:, 1:2]
                done(dve, "start" + kind, n)
                dve.tensor_tensor_scan(buf[:, ::-1], d, buf[:, ::-1], start, ALU.mult, ALU.add)\
                   .then_inc(st["y" + kind], 1)

            def step(n, p, wt=0, early=0, nxt=0, nxt3=0, late=0, out=0, outl=0, half=None, tail=0):
                m = n - LAG
                col = bass.ds(n, 1)
                E, V, U, W = ek[p][:, :], ekv[p][:, :], euk[p][:, :], wkv[1 - p][:, :]
                if early:
                    done(dve, "exps", n)
                    dve.tensor_scalar(E, E, E30, scl[:, col], ALU.min, ALU.mult).then_inc(st["clamp"], 1)
                    dve.scalar_tensor_tensor(own[p][:, :], U, E30, kT[:, :], ALU.min, ALU.mult)
                    done(dve, "clamp", n)
                    dve.tensor_tensor(V, E, kT[:, :], ALU.mult).then_inc(st["own"], 1)
                    forward(E, n, "clamp", "d")
                if wt:
                    landed(dve, w_in, n, p)
                    done(dve, "wT", n - 2)
                    dve.tensor_scalar(s_nat[p], w_nat[p][:, :], 0.0, SIGN, ALU.is_ge, ALU.subtract)\
                       .then_inc(st["sgn"], 1)
                if late and not out:
                    done(dve, "wTc", n - 1)
                    feats = bass.ds((n - 1) * P, P)
                    dve.tensor_scalar(sgn[:, 1, :, feats], sgn[:, 0, :, feats], 1.0 / LO_GAIN, None, ALU.mult)\
                       .then_inc(st["sgnl"], 1)
                if early and not wt and not out:
                    done(dve, "abs", CT - 1)
                    for b in range(B):
                        ins = dve.tensor_scalar(oscale[:, b * CT:(b + 1) * CT], asum[:, :], gain[:, b:b + 1],
                                                1.0 / (C * SIGN), ALU.mult, ALU.mult)
                    ins.then_inc(s_osc, 1)
                if early:
                    start_from(E, n, "d")
                    backward(E, n, "d")
                if late:
                    done(dve, "inv", n - 1)
                    done(dve, "num", n - 1)
                    dve.scalar_tensor_tensor(W, W, 1.0 / DEN_MIN, ekv[1 - p][:, :], ALU.min, ALU.mult)\
                       .then_inc(st["quot"], 1)
                if early:
                    done(dve, "yd", n)
                    dve.scalar_tensor_tensor(U, U, E30, E, ALU.min, ALU.add).then_inc(st["den"], 1)
                if late:
                    done(dve, "sT", n - 1)
                    done(dve, "quot", n - 1)
                    dve.scalar_tensor_tensor(W, W, HI_SCALE * LO_GAIN, sT[:, :], ALU.mult, ALU.mult)\
                       .then_inc(st["base"], 1)
                if early:
                    forward(V, n, "own", "n")
                    start_from(V, n, "n")
                    backward(V, n, "n")
                if outl and tail:
                    residual(m - 1, p, 0)
                if out and tail == PARTS:
                    done(dve, "prod", m)
                    dve.wait_ge(s_halfc, NPART)
                    done(dve, "yT1", m - 2)
                    dve.scalar_tensor_tensor(y_fm[1 - p][:, :], prods[p].rearrange("p h t -> p (h t)"),
                                             oscale[:, bass.ds(m, 1)],
                                             y_part[:, bass.ds(m - (N - CT), 1), :].rearrange("p a t -> p (a t)"),
                                             ALU.mult, ALU.add).then_inc(st["ev"], 1)
                if outl and tail:
                    residual(m - 1, p, 1)

            run(dve, step)


_INS = ["x", "fside_BxSxS_0", "cond_512", "L0_cond_w", "L0_cond_u", "L0_ffn_weight", "L0_ffn_bias"]
_OUTS = [((4, 1024, 1024), "float32")]


def kernel(**inputs):
    import numpy as _np
    import concourse.bacc as _bacc
    from concourse import mybir as _mybir
    from concourse.bass_utils import run_bass_kernel_spmd as _run

    nc = _bacc.Bacc("TRN2", target_bir_lowering=False, num_devices=1)
    arrays, args = {}, []
    for name in _INS:
        a = _np.ascontiguousarray(inputs[name])
        arrays[f"in_{name}_dram"] = a
        args.append(nc.dram_tensor(f"in_{name}_dram", a.shape, _mybir.dt.from_np(a.dtype), kind="ExternalInput").ap())
    for i, (shape, dtype) in enumerate(_OUTS):
        dt = _mybir.dt.from_np(_np.dtype(dtype))
        args.append(nc.dram_tensor(f"out_{i}_dram", shape, dt, kind="ExternalOutput").ap())
    bi_wkv_binary_ffn(nc, *args)
    r = _run(nc, [arrays], core_ids=[0])
    return r.results[0]["out_0_dram"]
```
